# Optimizing a Trainium2 kernel written in Bass

```python
import numpy as np
import jax
import jax.numpy as jnp

def _softmax(x, axis=-1):
    return jax.nn.softmax(x, axis=axis)
def _gelu(x):
    return jax.nn.gelu(x, approximate=True)
def _silu(x):
    return jax.nn.silu(x)
def _sigmoid(x):
    return jax.nn.sigmoid(x)
def _layernorm(x, axis=-1, eps=1e-5):
    m = jnp.mean(x, axis=axis, keepdims=True)
    v = jnp.var(x, axis=axis, keepdims=True)
    return (x - m) / jnp.sqrt(v + eps)
def _scatter_add(tgt, idx, src, axis=0):
    return tgt.at[idx].add(src)
def _segment_sum(src, seg, n):
    return jax.ops.segment_sum(src, seg, n)

kernel_name = 'mk_conv_preact_d1_conv_nchw32_7370de'

def setup_inputs(seed: int = 0):
    np.random.seed(seed)
    _w = jnp.asarray
    def _rec_inputs():
        import jax
        import jax.numpy as jnp
        _gk = jax.random.key(seed)
        x = 1.508e-05 + 1 * jax.random.normal(jax.random.fold_in(_gk, 1), (8, 32, 512, 512), jnp.float32)
        return x
    x = _rec_inputs()
    def _L0_conv_setup():
        import jax, jax.numpy as jnp
        import numpy as np
        LEVELS = 3

        def _wavelet_pyramid(x, levels=LEVELS):
            B, C, H, W = x.shape
            k1 = jnp.array([0.25, 0.5, 0.25], dtype=x.dtype)
            K = jnp.outer(k1, k1)[None, None]
            result = x
            for level in range(levels):
                sh, sw = (H // 2 ** level, W // 2 ** level)
                if min(sh, sw) <= 2:
                    break
                temp = result[:, :, :sh, :sw].reshape(B * C, 1, sh, sw)
                approx = jax.lax.conv_general_dilated(temp, K, window_strides=(1, 1), padding='SAME', dimension_numbers=('NCHW', 'OIHW', 'NCHW'))
                down = approx[:, :, ::2, ::2][:, :, :sh // 2, :sw // 2]
                result = result.at[:, :, :sh // 2, :sw // 2].set(down.reshape(B, C, sh // 2, sw // 2))
            return result
        key = jax.random.key(seed)
        x = jax.random.normal(key, (8, 32, 512, 512), dtype=jnp.float32)
        return {'x': x}
    _L0_conv_all = _L0_conv_setup()
    _L0_conv_in = {k: v for k, v in _L0_conv_all.items() if k in ()}
    del _L0_conv_all

    return {
        "x": x,
    }

def reference(x):
    import jax
    import jax.numpy as jnp
    def _L0_conv_ref(x):
        import jax, jax.numpy as jnp
        import numpy as np
        LEVELS = 3

        def _wavelet_pyramid(x, levels=LEVELS):
            B, C, H, W = x.shape
            k1 = jnp.array([0.25, 0.5, 0.25], dtype=x.dtype)
            K = jnp.outer(k1, k1)[None, None]
            result = x
            for level in range(levels):
                sh, sw = (H // 2 ** level, W // 2 ** level)
                if min(sh, sw) <= 2:
                    break
                temp = result[:, :, :sh, :sw].reshape(B * C, 1, sh, sw)
                approx = jax.lax.conv_general_dilated(temp, K, window_strides=(1, 1), padding='SAME', dimension_numbers=('NCHW', 'OIHW', 'NCHW'))
                down = approx[:, :, ::2, ::2][:, :, :sh // 2, :sw // 2]
                result = result.at[:, :, :sh // 2, :sw // 2].set(down.reshape(B, C, sh // 2, sw // 2))
            return result
        return _wavelet_pyramid(x, LEVELS)

    def _gn(v, G=16, eps=1e-5):
        B_, C_, H_, W_ = v.shape
        g = v.reshape(B_, G, C_ // G, H_, W_)
        m = jnp.mean(g, axis=(2, 3, 4), keepdims=True)
        s = jnp.var(g, axis=(2, 3, 4), keepdims=True)
        return ((g - m) / jnp.sqrt(s + eps)).reshape(v.shape)

    def _ln_c(v, eps=1e-6):
        m = jnp.mean(v, axis=1, keepdims=True)
        s = jnp.var(v, axis=1, keepdims=True)
        return (v - m) / jnp.sqrt(s + eps)

    def _ln_t(v, eps=1e-5):
        m = jnp.mean(v, axis=-1, keepdims=True)
        s = jnp.var(v, axis=-1, keepdims=True)
        return (v - m) / jnp.sqrt(s + eps)

    def _to_tokens(v):
        B_, C_, H_, W_ = v.shape
        return v.reshape(B_, C_, H_ * W_).transpose(0, 2, 1)
    def _from_tokens(t, like):
        B_, C_, H_, W_ = like.shape
        return t.transpose(0, 2, 1).reshape(B_, C_, H_, W_)

    x = x + _L0_conv_ref(_gn(x))
    return x


_drawn_inputs = setup_inputs


def setup_inputs(seed=0):
    import zlib

    import numpy as np

    out = dict(_drawn_inputs(seed))
    spreads = {}
    factors = {}
    for name, (base, spread) in spreads.items():
        noise = np.random.default_rng([zlib.crc32(name.encode()), seed]).standard_normal(out[name].shape)
        drawn = base * np.exp(spread * noise) if base else spread * noise
        out[name] = jnp.asarray(drawn.astype(out[name].dtype))
    for name, factor in factors.items():
        out[name] = (out[name] * factor).astype(out[name].dtype)
    return out
```

```python
from contextlib import ExitStack

import concourse.bass as bass
from concourse import mybir

F32 = mybir.dt.float32
BF16 = mybir.dt.bfloat16
ALU = mybir.AluOpType
ACT = mybir.ActivationFunctionType

P = 128
EPS = 1e-5
CG = 2
HALVES = 2
RPP = 2
SLOTS = 8
LAG_COEF = 1
LAG_L1 = 2
LAG_L2 = 3
AHEAD = 4


def pyramid_kernel(nc: bass.Bass, x: bass.AP, out: bass.AP):
    B, C, H, W = x.shape
    G = B * C // CG
    N = CG * H * W
    ROWS = CG * HALVES * RPP
    W1, W2, W3 = W // 2, W // 4, W // 8
    assert H == HALVES * RPP * P and G % SLOTS == 0 and G > SLOTS and CG * W1 <= 512

    def groups(a):
        return a.rearrange("b (g c) (f p s) w -> (b g) p c f (s w)", c=CG, f=HALVES, s=RPP)

    x_dram = groups(x).rearrange("(l k) p c f n -> l k p c f n", k=SLOTS)
    out_dram = groups(out)

    with ExitStack() as ctx:
        def sb(name, shape, dt=F32):
            return ctx.enter_context(nc.sbuf_tensor(name, shape, dt))

        def psum(name, shape):
            return ctx.enter_context(nc.psum_tensor(name, shape, F32))

        def sem(name):
            return ctx.enter_context(nc.semaphore(name))

        xs = sb("xs", [P, SLOTS, ROWS * W])
        h1 = sb("h1", [P, 2, ROWS, W1])
        a1 = sb("a1", [P, 2, CG * HALVES, W1])
        l1 = sb("l1", [P, 2, RPP, CG, W1])
        h2 = sb("h2", [P, 2, RPP * CG, W2])
        l2 = sb("l2", [P, 2, CG, W2])
        squares = sb("squares", [P, ROWS * W], BF16)
        hsum = sb("hsum", [P, 2])
        junk8 = sb("junk8", [P, ROWS])
        negm = sb("negm", [P, 2])
        sumsq = sb("sumsq", [P, 2])
        std = sb("std", [P, 2])
        ve = sb("ve", [P, 2])
        r0 = sb("r0", [P, 2])
        newt = sb("newt", [P, 2, 4])
        r = sb("r", [P, 2])
        r_plus1 = sb("r_plus1", [P, 2])
        negmr = sb("negmr", [P, 2])
        negmr_e = sb("negmr_e", [P, 2])
        top_even, top_odd, top_prev, bot_even, bot_odd, bot_prev = (
            sb(n, [P, P]) for n in ("top_even", "top_odd", "top_prev", "bot_even", "bot_odd", "bot_prev"))
        w2_first, w2_second = sb("w2_first", [P, P]), sb("w2_second", [P, P])
        w3_odd, w3_even, w3_keep = sb("w3_odd", [P, P]), sb("w3_even", [P, P]), sb("w3_keep", [P, P])
        mean_w, var_w = sb("mean_w", [P, P]), sb("var_w", [P, P])
        col_w = sb("col_w", [1, RPP, P])
        edge = sb("edge", [P, 2])
        three = sb("three", [P, 1])
        half_t = sb("half_t", [P, 1])
        eps_t = sb("eps_t", [P, 1])

        l1_ps = [psum(f"l1_ps{i}", [P, RPP, CG, W1]) for i in range(2)]
        l2_ps = [psum(f"l2_ps{i}", [P, 512]) for i in range(2)]
        mean_ps = psum("mean_ps", [P, 512])
        var_ps = psum("var_ps", [P, 512])

        x_loaded = [sem(f"x_loaded{i}") for i in range(SLOTS)]
        x_stored = [sem(f"x_stored{i}") for i in range(SLOTS)]
        consts_ready = sem("consts_ready")
        const_step = sem("const_step")
        h1_part = sem("h1_part")
        h1_ready = sem("h1_ready")
        a1_ready = sem("a1_ready")
        mean_ready = sem("mean_ready")
        negm_ready = sem("negm_ready")
        sumsq_ready = sem("sumsq_ready")
        var_ready = sem("var_ready")
        std_ready = sem("std_ready")
        r0_ready = sem("r0_ready")
        newt_step = sem("newt_step")
        coef_ready = sem("coef_ready")
        l1_ps_ready = sem("l1_ps_ready")
        l1_ready = sem("l1_ready")
        scaled = sem("scaled")
        h2_part = sem("h2_part")
        h2_ready = sem("h2_ready")
        l1_added = sem("l1_added")
        l2_ps_ready = sem("l2_ps_ready")
        l2_ready = sem("l2_ready")
        l3_ps_ready = sem("l3_ps_ready")
        l2_added = sem("l2_added")

        block = ctx.enter_context(nc.Block())

        LAPS = G // SLOTS
        HEAD = [(0, u) for u in range(SLOTS)]
        TAIL = [(LAPS, u) for u in range(LAG_L2)]

        def exists(base, k):
            return not isinstance(base, int) or 0 <= base + k < G

        def later(base, k, n):
            return not isinstance(base, int) or base + k >= n

        def rows(slot):
            return xs[:, slot, :].rearrange("p (r w) -> p r w", w=W)

        def image(slot):
            return xs[:, slot, :].rearrange("p (c f s w) -> p c f s w", c=CG, f=HALVES, s=RPP)

        def whole(slot):
            return xs[:, slot, :].rearrange("p (c f n) -> p c f n", c=CG, f=HALVES)

        @block.sync
        def _(sp):
            def load(lap, k):
                slot, lap = k % SLOTS, lap + k // SLOTS
                if later(lap, 0, 1):
                    sp.wait_ge(x_stored[slot], 16 * lap)
                sp.dma_start(whole(slot), x_dram[lap, slot]).then_inc(x_loaded[slot], 16)

            def step(lap, u):
                base = lap * SLOTS
                k = u - LAG_L2
                if exists(base, k):
                    sp.wait_ge(scaled, base + k + 1)
                    sp.wait_ge(l1_added, base + k + 1)
                    sp.wait_ge(l2_added, base + k + 1)
                    sp.dma_start(out_dram[base + k], whole(k % SLOTS)).then_inc(x_stored[k % SLOTS], 16)
                if exists(base, u + AHEAD) and later(base, u + AHEAD, SLOTS):
                    load(lap, u + AHEAD)

            for k in range(SLOTS):
                load(0, k)
            for lap, u in HEAD:
                step(lap, u)
            with sp.Fori(1, LAPS - 1) as lap:
                for u in range(SLOTS):
                    step(lap, u)
            for lap, u in [(LAPS - 1, u) for u in range(SLOTS)] + TAIL:
                step(lap, u)
            for slot in range(SLOTS):
                sp.wait_ge(x_stored[slot], 16 * (G // SLOTS))

        @block.gpsimd
        def _(pool):
            count = [0]

            def ordered(ins):
                count[0] += 1
                ins.then_inc(const_step, 1)
                pool.wait_ge(const_step, count[0])

            def place(view, base, pattern, fill, p_step=1):
                ordered(nc.gpsimd.affine_select(out=view, in_=view, compare_op=ALU.not_equal, fill=fill,
                                                base=base, pattern=pattern, channel_multiplier=p_step))

            def halves(w):
                return w[:].rearrange("p (s q) -> p s q", s=2)

            last = None
            for w in (top_even, top_odd, top_prev, bot_even, bot_odd, bot_prev, w2_first, w2_second,
                      w3_odd, w3_keep):
                last = nc.gpsimd.memset(w[:], 0.0)
            nc.gpsimd.memset(mean_w[:], -0.5 / N)
            nc.gpsimd.memset(var_w[:], 1.0 / N)
            nc.gpsimd.memset(col_w[:], -0.25)
            nc.gpsimd.memset(edge[:], 1.0)
            nc.gpsimd.memset(three[:], 3.0)
            nc.gpsimd.memset(half_t[:], 0.5)
            ordered(nc.gpsimd.memset(eps_t[:], EPS))
            half = P // 2
            place(top_even[:], 0, [[-2, P]], 1 / 16)
            place(top_odd[:], -1, [[-2, P]], 1 / 16)
            place(top_prev[:], 1, [[-2, P]], 1 / 16)
            place(bot_even[:], 2 * half, [[-2, P]], 1 / 16)
            place(bot_odd[:], 2 * half - 1, [[-2, P]], 1 / 16)
            place(bot_prev[:], 2 * half + 1, [[-2, P]], 1 / 16)
            place(halves(w2_first), 0, [[-1, 2], [-2, half]], 2 / 16)
            place(halves(w2_second), 0, [[-1, 2], [-2, half]], 1 / 16)
            place(halves(w2_second), 1, [[-1, 2], [-2, half]], 1 / 16)
            third = halves(w3_odd)[:, :, 0:half // 2]
            place(third, 0, [[-1, 2], [-2, half // 2]], 2 / 16)
            place(third, -half, [[-1, 2], [-2, half // 2]], 1 / 16)
            place(third, 1 - half, [[-1, 2], [-2, half // 2]], 1 / 16)
            place(w3_odd[:, 0:1], 1 - half, [[0, 1]], 0.0)
            place(halves(w3_keep)[:, :, half // 2:half], -half // 2, [[-half, 2], [-1, half // 2]], 1.0)
            ordered(nc.gpsimd.tensor_scalar(w3_even[:], w3_odd[:], 2.0, 0.0, ALU.mult, ALU.add))
            place(edge[:, 0:1], 0, [[0, 1]], 0.75)
            ordered(nc.gpsimd.tensor_scalar(col_w[:, 0, 0:1], col_w[:, 0, 0:1], 0.75, 0.0, ALU.mult, ALU.add))
            nc.gpsimd.memset(junk8[:], 0.0).then_inc(consts_ready, 1)

            def step(lap, u):
                base = lap * SLOTS
                k = u - LAG_COEF
                if not exists(base, k):
                    return
                b = k % 2
                c = slice(b, b + 1)
                n = base + k
                pool.wait_ge(r0_ready, n + 1)
                if later(base, k, 2):
                    pool.wait_ge(scaled, n - 1)
                nc.gpsimd.tensor_tensor(newt[:, b, 0:1], r0[:, c], r0[:, c], ALU.mult).then_inc(newt_step, 1)
                pool.wait_ge(newt_step, 5 * n + 1)
                nc.gpsimd.tensor_tensor(newt[:, b, 1:2], newt[:, b, 0:1], ve[:, c], ALU.mult).then_inc(newt_step, 1)
                pool.wait_ge(newt_step, 5 * n + 2)
                nc.gpsimd.tensor_tensor(newt[:, b, 3:4], r0[:, c], half_t[:], ALU.mult)
                nc.gpsimd.tensor_tensor(newt[:, b, 2:3], three[:], newt[:, b, 1:2], ALU.subtract).then_inc(newt_step, 1)
                pool.wait_ge(newt_step, 5 * n + 3)
                nc.gpsimd.tensor_tensor(r[:, c], newt[:, b, 3:4], newt[:, b, 2:3], ALU.mult).then_inc(newt_step, 1)
                pool.wait_ge(newt_step, 5 * n + 4)
                nc.gpsimd.tensor_tensor(negmr[:, c], negm[:, c], r[:, c], ALU.mult).then_inc(newt_step, 1)
                nc.gpsimd.tensor_tensor(r_plus1[:, c], r[:, c], edge[:, 1:2], ALU.add)
                pool.wait_ge(newt_step, 5 * n + 5)
                nc.gpsimd.tensor_tensor(negmr_e[:, c], negmr[:, c], edge[:, 0:1], ALU.mult).then_inc(coef_ready, 1)

            for lap, u in HEAD:
                step(lap, u)
            with pool.Fori(1, LAPS) as lap:
                for u in range(SLOTS):
                    step(lap, u)
            for lap, u in TAIL:
                step(lap, u)

        @block.vector
        def _(dve):
            def step(lap, u):
                base = lap * SLOTS
                b = u % 2
                k = u - LAG_COEF
                make = exists(base, u)
                if make:
                    dve.wait_ge(x_loaded[u], 16 * (lap + 1))
                    if later(base, u, 2):
                        dve.wait_ge(l1_ps_ready, base + u - 1)
                        dve.wait_ge(mean_ready, base + u - 1)
                    v = rows(u % SLOTS)
                    nc.vector.scalar_tensor_tensor(h1[:, b], v[:, :, 0:W:2], 2.0, v[:, :, 1:W:2], ALU.mult,
                                                   ALU.add).then_inc(h1_part, 1)
                if make:
                    dve.wait_ge(h1_part, base + u + 1)
                    nc.vector.scalar_tensor_tensor(h1[:, b, :, 1:W1], v[:, :, 1:W - 2:2], 1.0, h1[:, b, :, 1:W1],
                                                   ALU.mult, ALU.add,
                                                   accum_out=hsum[:, b:b + 1]).then_inc(h1_ready, 1)
                    dve.wait_ge(h1_ready, base + u + 1)
                    hp = h1[:, b].rearrange("p (i s) w -> p i s w", s=RPP)
                    nc.vector.scalar_tensor_tensor(a1[:, b], hp[:, :, 0], 2.0, hp[:, :, 1], ALU.mult,
                                                   ALU.add).then_inc(a1_ready, 1)
                if exists(base, k):
                    c = slice(k % 2, k % 2 + 1)
                    dve.wait_ge(std_ready, base + k + 1)
                    if later(base, k, 2):
                        dve.wait_ge(coef_ready, base + k - 1)
                    nc.vector.reciprocal(r0[:, c], std[:, c])
                    nc.vector.tensor_scalar(ve[:, c], var_ps[:, c], EPS, None, ALU.add).then_inc(r0_ready, 1)
                k = u - LAG_L2
                if exists(base, k):
                    dve.wait_ge(l3_ps_ready, base + k + 1)
                    img = image(k % SLOTS)
                    for s in range(RPP):
                        part = slice(P // 2 * s, P // 2 * (s + 1))
                        level = l2_ps[k % 2][part, 0:CG * W2].rearrange("p (c w) -> p c w", c=CG)
                        corner = img[0:P // 2, :, 0, s, 0:W2]
                        last = nc.vector.tensor_tensor(corner, level, corner, ALU.add)
                    last.then_inc(l2_added, 1)
                k = u - LAG_L1
                if exists(base, k):
                    c, slot = k % 2, k % SLOTS
                    l1v = l1[:, c].rearrange("p s c w -> p (s c) w")
                    dve.wait_ge(l1_ready, base + k + 1)
                    if later(base, k, 2):
                        dve.wait_ge(l2_ps_ready, base + k - 1)
                    nc.vector.scalar_tensor_tensor(h2[:, c], l1v[:, :, 0:W1:2], 2.0, l1v[:, :, 1:W1:2], ALU.mult,
                                                   ALU.add).then_inc(h2_part, 1)
                    img = image(slot)
                    l1c = l1[:, c].rearrange("p s c w -> p c s w")
                    right = img[:, :, 0, :, W2:W1]
                    nc.vector.tensor_tensor(right, l1c[:, :, :, W2:W1], right, ALU.add)
                    dve.wait_ge(h2_part, base + k + 1)
                    nc.vector.scalar_tensor_tensor(h2[:, c, :, 1:W2], l1v[:, :, 1:W1 - 2:2], 1.0,
                                                   h2[:, c, :, 1:W2], ALU.mult, ALU.add).then_inc(h2_ready, 1)
                    below = img[P // 2:P, :, 0, :, 0:W2]
                    nc.vector.tensor_tensor(below, l1c[P // 2:P, :, :, 0:W2], below, ALU.add).then_inc(l1_added, 1)

            for lap, u in HEAD:
                step(lap, u)
            with dve.Fori(1, LAPS) as lap:
                for u in range(SLOTS):
                    step(lap, u)
            for lap, u in TAIL:
                step(lap, u)

        @block.tensor
        def _(pe):
            pe.wait_ge(consts_ready, 1)

            def step(lap, u):
                base = lap * SLOTS
                k = u - LAG_L2
                if exists(base, k):
                    pe.wait_ge(l2_ready, base + k + 1)
                    src = l2[:, k % 2]
                    dst = l2_ps[k % 2][:, 0:CG * W2].rearrange("p (c w) -> p c w", c=CG)
                    nc.tensor.matmul(dst[:, :, 0:W3], w3_even[:], src[:, :, 0:W2:2], start=True, stop=False)
                    nc.tensor.matmul(dst[:, :, 0:W3], w3_odd[:], src[:, :, 1:W2:2], start=False, stop=False)
                    nc.tensor.matmul(dst[:, :, 1:W3], w3_odd[:], src[:, :, 1:W2 - 2:2], start=False, stop=False)
                    nc.tensor.matmul(dst[:, :, 0:W3], w3_keep[:], src[:, :, 0:W3], start=False,
                                     stop=True).then_inc(l3_ps_ready, 1)
                if exists(base, u):
                    b = u % 2
                    hv = h1[:, b].rearrange("p (c f s) w -> p c f s w", c=CG, f=HALVES)
                    av = a1[:, b].rearrange("p (c f) w -> p c f w", c=CG)
                    mean8 = mean_ps[:, ROWS * b:ROWS * (b + 1)]
                    pe.wait_ge(h1_ready, base + u + 1)
                    if later(base, u, 1):
                        pe.wait_ge(negm_ready, base + u)
                    nc.tensor.matmul(mean8, mean_w[:], h1[:, b, :, 0], start=True, stop=False)
                    nc.tensor.matmul(mean8, mean_w[:], rows(u % SLOTS)[:, :, W - 1], start=False, stop=False)
                    nc.tensor.matmul(mean8[:, 0:1], mean_w[:], hsum[:, b:b + 1], start=False,
                                     stop=True).then_inc(mean_ready, 1)
                    if later(base, u, 2):
                        pe.wait_ge(l1_ready, base + u - 1)
                    even, odd = l1_ps[b][:, 0], l1_ps[b][:, 1]
                    nc.tensor.matmul(even, top_prev[:], hv[:, :, 0, 1], start=True, stop=False)
                    nc.tensor.matmul(even, bot_prev[:], hv[:, :, 1, 1], start=False, stop=False)
                    nc.tensor.matmul(odd, top_even[:], hv[:, :, 0, 1], start=True, stop=False)
                    nc.tensor.matmul(odd, bot_even[:], hv[:, :, 1, 1], start=False, stop=False)
                    pe.wait_ge(a1_ready, base + u + 1)
                    nc.tensor.matmul(even, top_even[:], av[:, :, 0], start=False, stop=False)
                    nc.tensor.matmul(even, bot_even[:], av[:, :, 1], start=False, stop=False)
                    nc.tensor.matmul(odd, top_odd[:], av[:, :, 0], start=False, stop=False)
                    nc.tensor.matmul(odd, bot_odd[:], av[:, :, 1], start=False, stop=False)
                    pe.wait_ge(negm_ready, base + u + 1)
                    m2 = negm[0:1, b:b + 1].to_broadcast([1, CG])
                    nc.tensor.matmul(even[:, :, 0], col_w[:, 0, :], m2, start=False, stop=True)
                    nc.tensor.matmul(odd[:, :, 0], col_w[:, 1, :], m2, start=False,
                                     stop=True).then_inc(l1_ps_ready, 1)
                if exists(base, u):
                    b = u % 2
                    pe.wait_ge(sumsq_ready, base + u + 1)
                    if later(base, u, 1):
                        pe.wait_ge(r0_ready, base + u)
                    nc.tensor.matmul(var_ps[:, b:b + 1], var_w[:], sumsq[:, b:b + 1], start=True,
                                     stop=True).then_inc(var_ready, 1)
                k = u - LAG_L1
                if exists(base, k):
                    b = k % 2
                    pe.wait_ge(h2_ready, base + k + 1)
                    if later(base, k, 2):
                        pe.wait_ge(l2_added, base + k - 1)
                    dst = l2_ps[b][:, 0:CG * W2]
                    src = h2[:, b].rearrange("p (s c) w -> p s (c w)", s=RPP)
                    nc.tensor.matmul(dst, w2_first[:], src[:, 0], start=True, stop=False)
                    nc.tensor.matmul(dst, w2_second[:], src[:, 1], start=False, stop=True).then_inc(l2_ps_ready, 1)

            for lap, u in HEAD:
                step(lap, u)
            with pe.Fori(1, LAPS) as lap:
                for u in range(SLOTS):
                    step(lap, u)
            for lap, u in TAIL:
                step(lap, u)

        @block.scalar
        def _(act):
            act.wait_ge(consts_ready, 1)

            def step(lap, u):
                base = lap * SLOTS
                k = u - LAG_COEF
                if exists(base, k):
                    c = slice(k % 2, k % 2 + 1)
                    act.wait_ge(var_ready, base + k + 1)
                    if later(base, k, 2):
                        act.wait_ge(r0_ready, base + k - 1)
                    nc.scalar.activation(std[:, c], var_ps[:, c], ACT.Sqrt, bias=eps_t[:]).then_inc(std_ready, 1)
                k = u - LAG_L2
                if exists(base, k):
                    act.wait_ge(l2_ps_ready, base + k + 1)
                    if later(base, k, 2):
                        act.wait_ge(l3_ps_ready, base + k - 1)
                    nc.scalar.activation(l2[:, k % 2].rearrange("p c w -> p (c w)"), l2_ps[k % 2][:, 0:CG * W2],
                                         ACT.Identity).then_inc(l2_ready, 1)
                if exists(base, u):
                    b = u % 2
                    act.wait_ge(mean_ready, base + u + 1)
                    if later(base, u, 2):
                        act.wait_ge(coef_ready, base + u - 1)
                    nc.scalar.activation(junk8[:], mean_ps[:, ROWS * b:ROWS * (b + 1)], ACT.Identity,
                                         accum_out=negm[:, b:b + 1]).then_inc(negm_ready, 1)
                    act.wait_ge(negm_ready, base + u + 1)
                    if later(base, u, 2):
                        act.wait_ge(var_ready, base + u - 1)
                    nc.scalar.activation(squares[:], xs[:, u % SLOTS, :], ACT.Square, bias=negm[:, b:b + 1],
                                         accum_out=sumsq[:, b:b + 1]).then_inc(sumsq_ready, 1)
                k = u - LAG_COEF
                if exists(base, k):
                    b = k % 2
                    c = slice(b, b + 1)
                    act.wait_ge(coef_ready, base + k + 1)
                    act.wait_ge(l1_ps_ready, base + k + 1)
                    if later(base, k, 2):
                        act.wait_ge(l1_added, base + k - 1)
                    nc.scalar.activation(l1[:, b, 0], l1_ps[b][:, 0], ACT.Identity, bias=negmr_e[:, c],
                                         scale=r[:, c])
                    nc.scalar.activation(l1[:, b, 1], l1_ps[b][:, 1], ACT.Identity, bias=negmr[:, c],
                                         scale=r[:, c]).then_inc(l1_ready, 1)
                if exists(base, k):
                    img, halves = image(k % SLOTS), whole(k % SLOTS)
                    bottom, beside = halves[:, :, 1, :], img[:, :, 0, :, W1:W]
                    nc.scalar.activation(bottom, bottom, ACT.Identity, bias=negmr[:, c2(k)], scale=r_plus1[:, c2(k)])
                    nc.scalar.activation(beside, beside, ACT.Identity, bias=negmr[:, c2(k)],
                                         scale=r_plus1[:, c2(k)]).then_inc(scaled, 1)

            def c2(k):
                return slice(k % 2, k % 2 + 1)

            for lap, u in HEAD:
                step(lap, u)
            with act.Fori(1, LAPS) as lap:
                for u in range(SLOTS):
                    step(lap, u)
            for lap, u in TAIL:
                step(lap, u)


def kernel(x):
    import numpy as np
    import concourse.bacc as bacc
    from concourse.bass_utils import run_bass_kernel_spmd

    x = np.ascontiguousarray(x)
    nc = bacc.Bacc("TRN2", target_bir_lowering=False, num_devices=1)
    x_in = nc.dram_tensor("x_dram", x.shape, F32, kind="ExternalInput").ap()
    y_out = nc.dram_tensor("y_dram", x.shape, F32, kind="ExternalOutput").ap()
    pyramid_kernel(nc, x_in, y_out)
    r = run_bass_kernel_spmd(nc, [{"x_dram": x}], core_ids=[0])
    return r.results[0]["y_dram"]
```

```python
from contextlib import ExitStack

import concourse.bass as bass
from concourse import mybir

F32 = mybir.dt.float32
BF16 = mybir.dt.bfloat16
ALU = mybir.AluOpType
ACT = mybir.ActivationFunctionType

P = 128
EPS = 1e-5
CG = 2
HALVES = 2
RPP = 2
SLOTS = 8
LAG_COEF = 1
LAG_L1 = 2
LAG_L2 = 3
AHEAD = 4


def pyramid_kernel(nc: bass.Bass, x: bass.AP, out: bass.AP):
    B, C, H, W = x.shape
    G = B * C // CG
    N = CG * H * W
    ROWS = CG * HALVES * RPP
    W1, W2, W3 = W // 2, W // 4, W // 8
    assert H == HALVES * RPP * P and G % SLOTS == 0 and G > SLOTS and CG * W1 <= 512

    def groups(a):
        return a.rearrange("b (g c) (f p s) w -> (b g) p c f (s w)", c=CG, f=HALVES, s=RPP)

    x_dram = groups(x).rearrange("(l k) p c f n -> l k p c f n", k=SLOTS)
    out_dram = groups(out)

    with ExitStack() as ctx:
        def sb(name, shape, dt=F32):
            return ctx.enter_context(nc.sbuf_tensor(name, shape, dt))

        def psum(name, shape):
            return ctx.enter_context(nc.psum_tensor(name, shape, F32))

        def sem(name):
            return ctx.enter_context(nc.semaphore(name))

        xs = sb("xs", [P, SLOTS, ROWS * W])
        h1 = sb("h1", [P, 2, ROWS, W1])
        a1 = sb("a1", [P, 2, CG * HALVES, W1])
        l1 = sb("l1", [P, 2, RPP, CG, W1])
        h2 = sb("h2", [P, 2, RPP * CG, W2])
        l2 = sb("l2", [P, 2, CG, W2])
        squares = sb("squares", [P, ROWS * W], BF16)
        sums = sb("sums", [P, 2, ROWS + 1])
        junk9 = sb("junk9", [P, ROWS + 1])
        negm = sb("negm", [P, 2])
        sumsq = sb("sumsq", [P, 2])
        std = sb("std", [P, 2])
        ve = sb("ve", [P, 2])
        r0 = sb("r0", [P, 2])
        newt = sb("newt", [P, 2, 4])
        r = sb("r", [P, 2])
        r_plus1 = sb("r_plus1", [P, 2])
        negmr = sb("negmr", [P, 2])
        negmr_e = sb("negmr_e", [P, 2])
        col_fix = sb("col_fix", [P, 2, RPP])
        top_even, top_odd, top_prev, bot_even, bot_odd, bot_prev = (
            sb(n, [P, P]) for n in ("top_even", "top_odd", "top_prev", "bot_even", "bot_odd", "bot_prev"))
        w2_first, w2_second = sb("w2_first", [P, P]), sb("w2_second", [P, P])
        w3_odd, w3_even, w3_keep = sb("w3_odd", [P, P]), sb("w3_even", [P, P]), sb("w3_keep", [P, P])
        mean_w, var_w = sb("mean_w", [P, P]), sb("var_w", [P, P])
        edge = sb("edge", [P, 2])
        three = sb("three", [P, 1])
        half_t = sb("half_t", [P, 1])
        col_t = sb("col_t", [P, RPP])
        eps_t = sb("eps_t", [P, 1])

        l1_ps = [psum(f"l1_ps{i}", [P, RPP, CG, W1]) for i in range(2)]
        l2_ps = [psum(f"l2_ps{i}", [P, 512]) for i in range(2)]
        mean_ps = psum("mean_ps", [P, 512])
        var_ps = psum("var_ps", [P, 512])

        x_loaded = [sem(f"x_loaded{i}") for i in range(SLOTS)]
        x_stored = [sem(f"x_stored{i}") for i in range(SLOTS)]
        consts_ready = sem("consts_ready")
        const_step = sem("const_step")
        h1_part = sem("h1_part")
        h1_ready = sem("h1_ready")
        a1_ready = sem("a1_ready")
        sums_ready = sem("sums_ready")
        mean_ready = sem("mean_ready")
        negm_ready = sem("negm_ready")
        sumsq_ready = sem("sumsq_ready")
        var_ready = sem("var_ready")
        std_ready = sem("std_ready")
        r0_ready = sem("r0_ready")
        newt_step = sem("newt_step")
        coef_ready = sem("coef_ready")
        fix_ready = sem("fix_ready")
        l1_ps_ready = sem("l1_ps_ready")
        l1_ready = sem("l1_ready")
        l1_fixed = sem("l1_fixed")
        scaled = sem("scaled")
        h2_part = sem("h2_part")
        h2_ready = sem("h2_ready")
        l1_added = sem("l1_added")
        l2_ps_ready = sem("l2_ps_ready")
        l2_ready = sem("l2_ready")
        l3_ps_ready = sem("l3_ps_ready")
        l2_added = sem("l2_added")

        block = ctx.enter_context(nc.Block())

        LAPS = G // SLOTS
        HEAD = [(0, u) for u in range(SLOTS)]
        TAIL = [(LAPS, u) for u in range(LAG_L2)]

        def exists(base, k):
            return not isinstance(base, int) or 0 <= base + k < G

        def later(base, k, n):
            return not isinstance(base, int) or base + k >= n

        def rows(slot):
            return xs[:, slot, :].rearrange("p (r w) -> p r w", w=W)

        def image(slot):
            return xs[:, slot, :].rearrange("p (c f s w) -> p c f s w", c=CG, f=HALVES, s=RPP)

        def whole(slot):
            return xs[:, slot, :].rearrange("p (c f n) -> p c f n", c=CG, f=HALVES)

        @block.sync
        def _(sp):
            def load(lap, k):
                slot, lap = k % SLOTS, lap + k // SLOTS
                if later(lap, 0, 1):
                    sp.wait_ge(x_stored[slot], 16 * lap)
                sp.dma_start(whole(slot), x_dram[lap, slot]).then_inc(x_loaded[slot], 16)

            def step(lap, u):
                base = lap * SLOTS
                k = u - LAG_L2
                if exists(base, k):
                    sp.wait_ge(scaled, base + k + 1)
                    sp.wait_ge(l1_added, base + k + 1)
                    sp.wait_ge(l2_added, base + k + 1)
                    sp.dma_start(out_dram[base + k], whole(k % SLOTS)).then_inc(x_stored[k % SLOTS], 16)
                if exists(base, u + AHEAD) and later(base, u + AHEAD, SLOTS):
                    load(lap, u + AHEAD)

            for k in range(SLOTS):
                load(0, k)
            for lap, u in HEAD:
                step(lap, u)
            with sp.Fori(1, LAPS - 1) as lap:
                for u in range(SLOTS):
                    step(lap, u)
            for lap, u in [(LAPS - 1, u) for u in range(SLOTS)] + TAIL:
                step(lap, u)
            for slot in range(SLOTS):
                sp.wait_ge(x_stored[slot], 16 * (G // SLOTS))

        @block.gpsimd
        def _(pool):
            count = [0]

            def ordered(ins):
                count[0] += 1
                ins.then_inc(const_step, 1)
                pool.wait_ge(const_step, count[0])

            def place(view, base, pattern, fill, p_step=1):
                ordered(nc.gpsimd.affine_select(out=view, in_=view, compare_op=ALU.not_equal, fill=fill,
                                                base=base, pattern=pattern, channel_multiplier=p_step))

            def halves(w):
                return w[:].rearrange("p (s q) -> p s q", s=2)

            for w in (top_even, top_odd, top_prev, bot_even, bot_odd, bot_prev, w2_first, w2_second,
                      w3_odd, w3_keep):
                nc.gpsimd.memset(w[:], 0.0)
            nc.gpsimd.memset(mean_w[:], -0.5 / N)
            nc.gpsimd.memset(var_w[:], 1.0 / N)
            nc.gpsimd.memset(col_t[:], -0.25)
            nc.gpsimd.memset(edge[:], 1.0)
            nc.gpsimd.memset(three[:], 3.0)
            nc.gpsimd.memset(half_t[:], 0.5)
            ordered(nc.gpsimd.memset(eps_t[:], EPS))
            half = P // 2
            place(top_even[:], 0, [[-2, P]], 1 / 16)
            place(top_odd[:], -1, [[-2, P]], 1 / 16)
            place(top_prev[:], 1, [[-2, P]], 1 / 16)
            place(bot_even[:], 2 * half, [[-2, P]], 1 / 16)
            place(bot_odd[:], 2 * half - 1, [[-2, P]], 1 / 16)
            place(bot_prev[:], 2 * half + 1, [[-2, P]], 1 / 16)
            place(halves(w2_first), 0, [[-1, 2], [-2, half]], 2 / 16)
            place(halves(w2_second), 0, [[-1, 2], [-2, half]], 1 / 16)
            place(halves(w2_second), 1, [[-1, 2], [-2, half]], 1 / 16)
            third = halves(w3_odd)[:, :, 0:half // 2]
            place(third, 0, [[-1, 2], [-2, half // 2]], 2 / 16)
            place(third, -half, [[-1, 2], [-2, half // 2]], 1 / 16)
            place(third, 1 - half, [[-1, 2], [-2, half // 2]], 1 / 16)
            place(w3_odd[:, 0:1], 1 - half, [[0, 1]], 0.0)
            place(halves(w3_keep)[:, :, half // 2:half], -half // 2, [[-half, 2], [-1, half // 2]], 1.0)
            ordered(nc.gpsimd.tensor_scalar(w3_even[:], w3_odd[:], 2.0, 0.0, ALU.mult, ALU.add))
            place(edge[:, 0:1], 0, [[0, 1]], 0.75)
            ordered(nc.gpsimd.tensor_tensor(col_t[:, 0:1], col_t[:, 0:1], edge[:, 0:1], ALU.mult))
            nc.gpsimd.memset(junk9[:], 0.0).then_inc(consts_ready, 1)

            def step(lap, u):
                base = lap * SLOTS
                if exists(base, u):
                    b = u % 2
                    pool.wait_ge(h1_ready, base + u + 1)
                    if later(base, u, 2):
                        pool.wait_ge(mean_ready, base + u - 1)
                    nc.gpsimd.tensor_tensor(sums[:, b, 0:ROWS], h1[:, b, :, 0], rows(u)[:, :, W - 1],
                                            ALU.add).then_inc(sums_ready, 1)
                k = u - LAG_COEF
                if exists(base, k):
                    b = k % 2
                    c = slice(b, b + 1)
                    n = base + k
                    pool.wait_ge(r0_ready, n + 1)
                    if later(base, k, 2):
                        pool.wait_ge(scaled, n - 1)
                    nc.gpsimd.tensor_tensor(newt[:, b, 0:1], r0[:, c], r0[:, c], ALU.mult).then_inc(newt_step, 1)
                    nc.gpsimd.tensor_tensor(newt[:, b, 3:4], r0[:, c], half_t[:], ALU.mult)
                    pool.wait_ge(newt_step, 5 * n + 1)
                    nc.gpsimd.tensor_tensor(newt[:, b, 1:2], newt[:, b, 0:1], ve[:, c], ALU.mult).then_inc(newt_step, 1)
                    pool.wait_ge(newt_step, 5 * n + 2)
                    nc.gpsimd.tensor_tensor(newt[:, b, 2:3], three[:], newt[:, b, 1:2],
                                            ALU.subtract).then_inc(newt_step, 1)
                    pool.wait_ge(newt_step, 5 * n + 3)
                    nc.gpsimd.tensor_tensor(r[:, c], newt[:, b, 3:4], newt[:, b, 2:3], ALU.mult).then_inc(newt_step, 1)
                    pool.wait_ge(newt_step, 5 * n + 4)
                    nc.gpsimd.tensor_tensor(negmr[:, c], negm[:, c], r[:, c], ALU.mult).then_inc(newt_step, 1)
                    nc.gpsimd.tensor_tensor(r_plus1[:, c], r[:, c], edge[:, 1:2], ALU.add)
                    pool.wait_ge(newt_step, 5 * n + 5)
                    nc.gpsimd.tensor_tensor(negmr_e[:, c], negmr[:, c], edge[:, 0:1], ALU.mult).then_inc(coef_ready, 1)
                    nc.gpsimd.tensor_tensor(col_fix[:, b], negmr[:, c].to_broadcast([P, RPP]), col_t[:],
                                            ALU.mult).then_inc(fix_ready, 1)
                    pool.wait_ge(fix_ready, n + 1)
                    pool.wait_ge(l1_ready, n + 1)
                    for ch in range(CG):
                        col = l1[:, b, :, ch, 0]
                        last = nc.gpsimd.tensor_tensor(col, col, col_fix[:, b], ALU.add)
                    last.then_inc(l1_fixed, 1)

            for lap, u in HEAD:
                step(lap, u)
            with pool.Fori(1, LAPS) as lap:
                for u in range(SLOTS):
                    step(lap, u)
            for lap, u in TAIL:
                step(lap, u)

        @block.vector
        def _(dve):
            def step(lap, u):
                base = lap * SLOTS
                b = u % 2
                k = u - LAG_COEF
                make = exists(base, u)
                if make:
                    dve.wait_ge(x_loaded[u], 16 * (lap + 1))
                    if later(base, u, 2):
                        dve.wait_ge(l1_ps_ready, base + u - 1)
                        dve.wait_ge(mean_ready, base + u - 1)
                    v = rows(u)
                    nc.vector.scalar_tensor_tensor(h1[:, b], v[:, :, 0:W:2], 2.0, v[:, :, 1:W:2], ALU.mult,
                                                   ALU.add).then_inc(h1_part, 1)
                m = u - LAG_L1
                second = exists(base, m)
                if second:
                    c = m % 2
                    l1v = l1[:, c].rearrange("p s c w -> p (s c) w")
                    dve.wait_ge(l1_fixed, base + m + 1)
                    if later(base, m, 2):
                        dve.wait_ge(l2_ps_ready, base + m - 1)
                    nc.vector.scalar_tensor_tensor(h2[:, c], l1v[:, :, 0:W1:2], 2.0, l1v[:, :, 1:W1:2], ALU.mult,
                                                   ALU.add).then_inc(h2_part, 1)
                if make:
                    dve.wait_ge(h1_part, base + u + 1)
                    nc.vector.scalar_tensor_tensor(h1[:, b, :, 1:W1], v[:, :, 1:W - 2:2], 1.0, h1[:, b, :, 1:W1],
                                                   ALU.mult, ALU.add,
                                                   accum_out=sums[:, b, ROWS:ROWS + 1]).then_inc(h1_ready, 1)
                if second:
                    dve.wait_ge(h2_part, base + m + 1)
                    nc.vector.scalar_tensor_tensor(h2[:, c, :, 1:W2], l1v[:, :, 1:W1 - 2:2], 1.0,
                                                   h2[:, c, :, 1:W2], ALU.mult, ALU.add).then_inc(h2_ready, 1)
                if make:
                    dve.wait_ge(h1_ready, base + u + 1)
                    hp = h1[:, b].rearrange("p (i s) w -> p i s w", s=RPP)
                    nc.vector.scalar_tensor_tensor(a1[:, b], hp[:, :, 0], 2.0, hp[:, :, 1], ALU.mult,
                                                   ALU.add).then_inc(a1_ready, 1)
                if exists(base, k):
                    d = slice(k % 2, k % 2 + 1)
                    dve.wait_ge(std_ready, base + k + 1)
                    if later(base, k, 2):
                        dve.wait_ge(coef_ready, base + k - 1)
                    nc.vector.reciprocal(r0[:, d], std[:, d])
                    nc.vector.tensor_scalar(ve[:, d], var_ps[:, d], EPS, None, ALU.add).then_inc(r0_ready, 1)
                if second:
                    img = image(m % SLOTS)
                    l1c = l1[:, c].rearrange("p s c w -> p c s w")
                    right, below = img[:, :, 0, :, W2:W1], img[P // 2:P, :, 0, :, 0:W2]
                    nc.vector.tensor_tensor(right, l1c[:, :, :, W2:W1], right, ALU.add)
                    nc.vector.tensor_tensor(below, l1c[P // 2:P, :, :, 0:W2], below, ALU.add).then_inc(l1_added, 1)
                k = u - LAG_L2
                if exists(base, k):
                    dve.wait_ge(l3_ps_ready, base + k + 1)
                    img = image(k % SLOTS)
                    for s in range(RPP):
                        part = slice(P // 2 * s, P // 2 * (s + 1))
                        level = l2_ps[k % 2][part, 0:CG * W2].rearrange("p (c w) -> p c w", c=CG)
                        corner = img[0:P // 2, :, 0, s, 0:W2]
                        last = nc.vector.tensor_tensor(corner, level, corner, ALU.add)
                    last.then_inc(l2_added, 1)

            for lap, u in HEAD:
                step(lap, u)
            with dve.Fori(1, LAPS) as lap:
                for u in range(SLOTS):
                    step(lap, u)
            for lap, u in TAIL:
                step(lap, u)

        @block.tensor
        def _(pe):
            pe.wait_ge(consts_ready, 1)

            def step(lap, u):
                base = lap * SLOTS
                b = u % 2
                make = exists(base, u)
                if make:
                    hv = h1[:, b].rearrange("p (c f s) w -> p c f s w", c=CG, f=HALVES)
                    av = a1[:, b].rearrange("p (c f) w -> p c f w", c=CG)
                    pe.wait_ge(sums_ready, base + u + 1)
                    pe.wait_ge(h1_ready, base + u + 1)
                    if later(base, u, 1):
                        pe.wait_ge(negm_ready, base + u)
                    nc.tensor.matmul(mean_ps[:, 16 * b:16 * b + ROWS + 1], mean_w[:], sums[:, b], start=True,
                                     stop=True).then_inc(mean_ready, 1)
                    if later(base, u, 2):
                        pe.wait_ge(l1_ready, base + u - 1)
                    even, odd = l1_ps[b][:, 0], l1_ps[b][:, 1]
                    nc.tensor.matmul(even, top_prev[:], hv[:, :, 0, 1], start=True, stop=False)
                    nc.tensor.matmul(even, bot_prev[:], hv[:, :, 1, 1], start=False, stop=False)
                k = u - LAG_L2
                if exists(base, k):
                    pe.wait_ge(l2_ready, base + k + 1)
                    src = l2[:, k % 2]
                    dst = l2_ps[k % 2][:, 0:CG * W2].rearrange("p (c w) -> p c w", c=CG)
                    nc.tensor.matmul(dst[:, :, 0:W3], w3_even[:], src[:, :, 0:W2:2], start=True, stop=False)
                    nc.tensor.matmul(dst[:, :, 0:W3], w3_odd[:], src[:, :, 1:W2:2], start=False, stop=False)
                    nc.tensor.matmul(dst[:, :, 1:W3], w3_odd[:], src[:, :, 1:W2 - 2:2], start=False, stop=False)
                    nc.tensor.matmul(dst[:, :, 0:W3], w3_keep[:], src[:, :, 0:W3], start=False,
                                     stop=True).then_inc(l3_ps_ready, 1)
                if make:
                    nc.tensor.matmul(odd, top_even[:], hv[:, :, 0, 1], start=True, stop=False)
                    nc.tensor.matmul(odd, bot_even[:], hv[:, :, 1, 1], start=False, stop=False)
                    pe.wait_ge(a1_ready, base + u + 1)
                    nc.tensor.matmul(even, top_even[:], av[:, :, 0], start=False, stop=False)
                    nc.tensor.matmul(even, bot_even[:], av[:, :, 1], start=False, stop=True)
                    nc.tensor.matmul(odd, top_odd[:], av[:, :, 0], start=False, stop=False)
                    nc.tensor.matmul(odd, bot_odd[:], av[:, :, 1], start=False,
                                     stop=True).then_inc(l1_ps_ready, 1)
                    pe.wait_ge(sumsq_ready, base + u + 1)
                    if later(base, u, 1):
                        pe.wait_ge(r0_ready, base + u)
                    nc.tensor.matmul(var_ps[:, b:b + 1], var_w[:], sumsq[:, b:b + 1], start=True,
                                     stop=True).then_inc(var_ready, 1)
                k = u - LAG_L1
                if exists(base, k):
                    b = k % 2
                    pe.wait_ge(h2_ready, base + k + 1)
                    if later(base, k, 2):
                        pe.wait_ge(l2_added, base + k - 1)
                    dst = l2_ps[b][:, 0:CG * W2]
                    src = h2[:, b].rearrange("p (s c) w -> p s (c w)", s=RPP)
                    nc.tensor.matmul(dst, w2_first[:], src[:, 0], start=True, stop=False)
                    nc.tensor.matmul(dst, w2_second[:], src[:, 1], start=False, stop=True).then_inc(l2_ps_ready, 1)

            for lap, u in HEAD:
                step(lap, u)
            with pe.Fori(1, LAPS) as lap:
                for u in range(SLOTS):
                    step(lap, u)
            for lap, u in TAIL:
                step(lap, u)

        @block.scalar
        def _(act):
            act.wait_ge(consts_ready, 1)

            def step(lap, u):
                base = lap * SLOTS
                k = u - LAG_COEF
                if exists(base, k):
                    c = slice(k % 2, k % 2 + 1)
                    act.wait_ge(var_ready, base + k + 1)
                    if later(base, k, 2):
                        act.wait_ge(r0_ready, base + k - 1)
                    nc.scalar.activation(std[:, c], var_ps[:, c], ACT.Sqrt, bias=eps_t[:]).then_inc(std_ready, 1)
                k = u - LAG_L2
                if exists(base, k):
                    act.wait_ge(l2_ps_ready, base + k + 1)
                    if later(base, k, 2):
                        act.wait_ge(l3_ps_ready, base + k - 1)
                    nc.scalar.activation(l2[:, k % 2].rearrange("p c w -> p (c w)"), l2_ps[k % 2][:, 0:CG * W2],
                                         ACT.Identity).then_inc(l2_ready, 1)
                if exists(base, u):
                    b = u % 2
                    act.wait_ge(mean_ready, base + u + 1)
                    if later(base, u, 2):
                        act.wait_ge(coef_ready, base + u - 1)
                    nc.scalar.activation(junk9[:], mean_ps[:, 16 * b:16 * b + ROWS + 1], ACT.Identity,
                                         accum_out=negm[:, b:b + 1]).then_inc(negm_ready, 1)
                    act.wait_ge(negm_ready, base + u + 1)
                    if later(base, u, 2):
                        act.wait_ge(var_ready, base + u - 1)
                    nc.scalar.activation(squares[:], xs[:, u % SLOTS, :], ACT.Square, bias=negm[:, b:b + 1],
                                         accum_out=sumsq[:, b:b + 1]).then_inc(sumsq_ready, 1)
                k = u - LAG_COEF
                if exists(base, k):
                    b = k % 2
                    c = slice(b, b + 1)
                    act.wait_ge(coef_ready, base + k + 1)
                    act.wait_ge(l1_ps_ready, base + k + 1)
                    if later(base, k, 2):
                        act.wait_ge(l1_added, base + k - 1)
                    nc.scalar.activation(l1[:, b, 0], l1_ps[b][:, 0], ACT.Identity, bias=negmr_e[:, c],
                                         scale=r[:, c])
                    nc.scalar.activation(l1[:, b, 1], l1_ps[b][:, 1], ACT.Identity, bias=negmr[:, c],
                                         scale=r[:, c]).then_inc(l1_ready, 1)
                    img, halves = image(k % SLOTS), whole(k % SLOTS)
                    bottom, beside = halves[:, :, 1, :], img[:, :, 0, :, W1:W]
                    nc.scalar.activation(bottom, bottom, ACT.Identity, bias=negmr[:, c], scale=r_plus1[:, c])
                    nc.scalar.activation(beside, beside, ACT.Identity, bias=negmr[:, c],
                                         scale=r_plus1[:, c]).then_inc(scaled, 1)

            for lap, u in HEAD:
                step(lap, u)
            with act.Fori(1, LAPS) as lap:
                for u in range(SLOTS):
                    step(lap, u)
            for lap, u in TAIL:
                step(lap, u)


def kernel(x):
    import numpy as np
    import concourse.bacc as bacc
    from concourse.bass_utils import run_bass_kernel_spmd

    x = np.ascontiguousarray(x)
    nc = bacc.Bacc("TRN2", target_bir_lowering=False, num_devices=1)
    x_in = nc.dram_tensor("x_dram", x.shape, F32, kind="ExternalInput").ap()
    y_out = nc.dram_tensor("y_dram", x.shape, F32, kind="ExternalOutput").ap()
    pyramid_kernel(nc, x_in, y_out)
    r = run_bass_kernel_spmd(nc, [{"x_dram": x}], core_ids=[0])
    return r.results[0]["y_dram"]
```
